# Optimizing a Trainium2 kernel written in Bass

```python
import numpy as np
import jax
import jax.numpy as jnp

def _softmax(x, axis=-1):
    return jax.nn.softmax(x, axis=axis)

def _gelu(x):
    return jax.nn.gelu(x, approximate=True)

def _silu(x):
    return jax.nn.silu(x)

def _sigmoid(x):
    return jax.nn.sigmoid(x)

def _layernorm(x, axis=-1, eps=1e-05):
    m = jnp.mean(x, axis=axis, keepdims=True)
    v = jnp.var(x, axis=axis, keepdims=True)
    return (x - m) / jnp.sqrt(v + eps)

def _scatter_add(tgt, idx, src, axis=0):
    return tgt.at[idx].add(src)

def _segment_sum(src, seg, n):
    return jax.ops.segment_sum(src, seg, n)
kernel_name = 'mk_dlrm_tower_d1_rec_r8_fac55b'

def setup_inputs(seed: int=0):
    np.random.seed(seed)
    _w = jnp.asarray

    def _rec_inputs():
        import jax
        import jax.numpy as jnp
        _tk = jax.random.key(seed)
        ids = jnp.stack([jax.random.randint(jax.random.fold_in(_tk, 200 + f), (512,), 0, v, jnp.int32) for f, v in enumerate([12500, 1250, 125000, 1250, 12500, 12500, 1000, 1250, 1250, 1250, 12500, 1250, 1000, 1000, 1250, 12500, 1250, 1000, 12500, 1250, 1000, 1250, 1000, 1250, 1000, 12500])], axis=1)
        tbl_0 = 0.05 * jax.random.normal(jax.random.fold_in(_tk, 500 + 0), (12500, 128), jnp.float32)
        tbl_1 = 0.05 * jax.random.normal(jax.random.fold_in(_tk, 500 + 1), (1250, 128), jnp.float32)
        tbl_2 = 0.05 * jax.random.normal(jax.random.fold_in(_tk, 500 + 2), (125000, 128), jnp.float32)
        tbl_3 = 0.05 * jax.random.normal(jax.random.fold_in(_tk, 500 + 3), (1250, 128), jnp.float32)
        tbl_4 = 0.05 * jax.random.normal(jax.random.fold_in(_tk, 500 + 4), (12500, 128), jnp.float32)
        tbl_5 = 0.05 * jax.random.normal(jax.random.fold_in(_tk, 500 + 5), (12500, 128), jnp.float32)
        tbl_6 = 0.05 * jax.random.normal(jax.random.fold_in(_tk, 500 + 6), (1000, 128), jnp.float32)
        tbl_7 = 0.05 * jax.random.normal(jax.random.fold_in(_tk, 500 + 7), (1250, 128), jnp.float32)
        tbl_8 = 0.05 * jax.random.normal(jax.random.fold_in(_tk, 500 + 8), (1250, 128), jnp.float32)
        tbl_9 = 0.05 * jax.random.normal(jax.random.fold_in(_tk, 500 + 9), (1250, 128), jnp.float32)
        tbl_10 = 0.05 * jax.random.normal(jax.random.fold_in(_tk, 500 + 10), (12500, 128), jnp.float32)
        tbl_11 = 0.05 * jax.random.normal(jax.random.fold_in(_tk, 500 + 11), (1250, 128), jnp.float32)
        tbl_12 = 0.05 * jax.random.normal(jax.random.fold_in(_tk, 500 + 12), (1000, 128), jnp.float32)
        tbl_13 = 0.05 * jax.random.normal(jax.random.fold_in(_tk, 500 + 13), (1000, 128), jnp.float32)
        tbl_14 = 0.05 * jax.random.normal(jax.random.fold_in(_tk, 500 + 14), (1250, 128), jnp.float32)
        tbl_15 = 0.05 * jax.random.normal(jax.random.fold_in(_tk, 500 + 15), (12500, 128), jnp.float32)
        tbl_16 = 0.05 * jax.random.normal(jax.random.fold_in(_tk, 500 + 16), (1250, 128), jnp.float32)
        tbl_17 = 0.05 * jax.random.normal(jax.random.fold_in(_tk, 500 + 17), (1000, 128), jnp.float32)
        tbl_18 = 0.05 * jax.random.normal(jax.random.fold_in(_tk, 500 + 18), (12500, 128), jnp.float32)
        tbl_19 = 0.05 * jax.random.normal(jax.random.fold_in(_tk, 500 + 19), (1250, 128), jnp.float32)
        tbl_20 = 0.05 * jax.random.normal(jax.random.fold_in(_tk, 500 + 20), (1000, 128), jnp.float32)
        tbl_21 = 0.05 * jax.random.normal(jax.random.fold_in(_tk, 500 + 21), (1250, 128), jnp.float32)
        tbl_22 = 0.05 * jax.random.normal(jax.random.fold_in(_tk, 500 + 22), (1000, 128), jnp.float32)
        tbl_23 = 0.05 * jax.random.normal(jax.random.fold_in(_tk, 500 + 23), (1250, 128), jnp.float32)
        tbl_24 = 0.05 * jax.random.normal(jax.random.fold_in(_tk, 500 + 24), (1000, 128), jnp.float32)
        tbl_25 = 0.05 * jax.random.normal(jax.random.fold_in(_tk, 500 + 25), (12500, 128), jnp.float32)
        _rk = jax.random.fold_in(_tk, 7)
        r_dense_features = -0.000520686 + 1.00062 * jax.random.normal(jax.random.fold_in(_rk, 101), (512, 128), jnp.float32)
        W_top1 = 0.0405887 * jax.random.normal(jax.random.fold_in(_tk, 801), (607, 512), jnp.float32)
        W_top2 = 0.0441942 * jax.random.normal(jax.random.fold_in(_tk, 802), (512, 256), jnp.float32)
        W_top3 = 0.0625 * jax.random.normal(jax.random.fold_in(_tk, 803), (256, 1), jnp.float32)
        b_top1 = jnp.zeros((512,), jnp.float32)
        b_top2 = jnp.zeros((256,), jnp.float32)
        return (r_dense_features, ids, tbl_0, tbl_1, tbl_2, tbl_3, tbl_4, tbl_5, tbl_6, tbl_7, tbl_8, tbl_9, tbl_10, tbl_11, tbl_12, tbl_13, tbl_14, tbl_15, tbl_16, tbl_17, tbl_18, tbl_19, tbl_20, tbl_21, tbl_22, tbl_23, tbl_24, tbl_25, W_top1, b_top1, W_top2, b_top2, W_top3)
    r_dense_features, ids, tbl_0, tbl_1, tbl_2, tbl_3, tbl_4, tbl_5, tbl_6, tbl_7, tbl_8, tbl_9, tbl_10, tbl_11, tbl_12, tbl_13, tbl_14, tbl_15, tbl_16, tbl_17, tbl_18, tbl_19, tbl_20, tbl_21, tbl_22, tbl_23, tbl_24, tbl_25, W_top1, b_top1, W_top2, b_top2, W_top3 = _rec_inputs()

    def _L0_rec_setup():
        import jax, jax.numpy as jnp
        import numpy as np
        F = 26
        N = F + 1
        _TRIU_I, _TRIU_J = np.triu_indices(N, k=1)
        key = jax.random.key(seed)
        k1, k2 = jax.random.split(key)
        B, D = (2048, 128)
        dense_features = jax.random.normal(k1, (B, D), dtype=jnp.float32)
        sparse_features = jax.random.normal(k2, (B, F, D), dtype=jnp.float32)
        return {'dense_features': dense_features, 'sparse_features': sparse_features}
    _L0_rec_all = _L0_rec_setup()
    _L0_rec_in = {k: v for k, v in _L0_rec_all.items() if k in ()}
    del _L0_rec_all
    return {'r_dense_features': r_dense_features, 'ids': ids, 'tbl_0': tbl_0, 'tbl_1': tbl_1, 'tbl_2': tbl_2, 'tbl_3': tbl_3, 'tbl_4': tbl_4, 'tbl_5': tbl_5, 'tbl_6': tbl_6, 'tbl_7': tbl_7, 'tbl_8': tbl_8, 'tbl_9': tbl_9, 'tbl_10': tbl_10, 'tbl_11': tbl_11, 'tbl_12': tbl_12, 'tbl_13': tbl_13, 'tbl_14': tbl_14, 'tbl_15': tbl_15, 'tbl_16': tbl_16, 'tbl_17': tbl_17, 'tbl_18': tbl_18, 'tbl_19': tbl_19, 'tbl_20': tbl_20, 'tbl_21': tbl_21, 'tbl_22': tbl_22, 'tbl_23': tbl_23, 'tbl_24': tbl_24, 'tbl_25': tbl_25, 'W_top1': W_top1, 'b_top1': b_top1, 'W_top2': W_top2, 'b_top2': b_top2, 'W_top3': W_top3}

def reference(r_dense_features, ids, tbl_0, tbl_1, tbl_2, tbl_3, tbl_4, tbl_5, tbl_6, tbl_7, tbl_8, tbl_9, tbl_10, tbl_11, tbl_12, tbl_13, tbl_14, tbl_15, tbl_16, tbl_17, tbl_18, tbl_19, tbl_20, tbl_21, tbl_22, tbl_23, tbl_24, tbl_25, W_top1, b_top1, W_top2, b_top2, W_top3):
    import jax
    import jax.numpy as jnp

    def _L0_rec_ref(dense_features, sparse_features):
        import jax, jax.numpy as jnp
        import numpy as np
        F = 26
        N = F + 1
        _TRIU_I, _TRIU_J = np.triu_indices(N, k=1)
        combined = jnp.concatenate([dense_features[:, None, :], sparse_features], axis=1)
        interactions = jnp.einsum('bnd,bmd->bnm', combined, combined)
        interactions_flat = interactions[:, _TRIU_I, _TRIU_J]
        return jnp.concatenate([dense_features, interactions_flat], axis=1)
    e = jnp.stack([tbl_0[ids[:, 0]], tbl_1[ids[:, 1]], tbl_2[ids[:, 2]], tbl_3[ids[:, 3]], tbl_4[ids[:, 4]], tbl_5[ids[:, 5]], tbl_6[ids[:, 6]], tbl_7[ids[:, 7]], tbl_8[ids[:, 8]], tbl_9[ids[:, 9]], tbl_10[ids[:, 10]], tbl_11[ids[:, 11]], tbl_12[ids[:, 12]], tbl_13[ids[:, 13]], tbl_14[ids[:, 14]], tbl_15[ids[:, 15]], tbl_16[ids[:, 16]], tbl_17[ids[:, 17]], tbl_18[ids[:, 18]], tbl_19[ids[:, 19]], tbl_20[ids[:, 20]], tbl_21[ids[:, 21]], tbl_22[ids[:, 22]], tbl_23[ids[:, 23]], tbl_24[ids[:, 24]], tbl_25[ids[:, 25]]], axis=1)
    z = _L0_rec_ref(r_dense_features, e)
    z = z.reshape(z.shape[0], -1)
    h = jnp.concatenate([z, r_dense_features], axis=1)
    h = jnp.maximum(h @ W_top1 + b_top1, 0.0)
    h = jnp.maximum(h @ W_top2 + b_top2, 0.0)
    y = h @ W_top3
    return y

_drawn_inputs = setup_inputs


def setup_inputs(seed=0):
    import zlib

    import numpy as np

    out = dict(_drawn_inputs(seed))
    spreads = {'b_top1': (0.0, 0.1), 'b_top2': (0.0, 0.1)}
    factors = {}
    for name, (base, spread) in spreads.items():
        noise = np.random.default_rng([zlib.crc32(name.encode()), seed]).standard_normal(out[name].shape)
        drawn = base * np.exp(spread * noise) if base else spread * noise
        out[name] = jnp.asarray(drawn.astype(out[name].dtype))
    for name, factor in factors.items():
        out[name] = (out[name] * factor).astype(out[name].dtype)
    return out
```

```python
from contextlib import ExitStack

import concourse.bass as bass
from concourse import mybir

P = 128
ALU = mybir.AluOpType
ACT = mybir.ActivationFunctionType
F32 = mybir.dt.float32
F32R = mybir.dt.float32r
I32 = mybir.dt.int32

Q = 4
QP = P // Q
LINE = 4
SAMPLES = 4
SLOT = P
PARTS = 4
CHUNKS = 8
DVE_CHUNKS = (2, 5)
PICKED = 6
RAW = 3


def dlrm_tower(nc, dense, ids, tables, W1, b1, W2, b2, W3, out):
    B, D = dense.shape
    F = len(tables)
    N = F + 1
    H1 = W1.shape[1]
    H2 = W2.shape[1]
    TILES = B // P
    M1, M2 = H1 // P, H2 // P
    GROUPS = P // SAMPLES // PARTS
    HB = P // PARTS

    picked = [f for f in range(F) if tables[f].shape[0] <= CHUNKS * P and tables[f].shape[0] % CHUNKS == 0][-PICKED:]
    A = len(picked)
    K = tables[picked[0]].shape[0] // CHUNKS
    assert all(tables[f].shape[0] == K * CHUNKS for f in picked)
    gathered_tables = [f for f in range(F) if f not in picked]
    turned_features = [0] + [1 + f for f in gathered_tables]
    lines = [turned_features[i:i + LINE] for i in range(0, len(turned_features), LINE)]
    LINES = len(lines)

    COPIES = 2
    AT = COPIES
    COLS = N - 1
    T4 = (COLS - COPIES) // Q
    assert D == P and N + COPIES <= QP and T4 * Q == COLS - COPIES
    assert W1.shape[0] == 2 * D + N * (N - 1) // 2

    def first_pair_row(j):
        return D + j * N - j * (j + 1) // 2

    def runs(features):
        found, i = [], 0
        while i < len(features):
            step = features[i + 1] - features[i] if i + 1 < len(features) else 1
            n = 1
            while i + n < len(features) and features[i + n] == features[i] + n * step:
                n += 1
            if n == 2 and step > 1 and i + 2 < len(features):
                n, step = 1, 1
            found.append((i, features[i], step, n))
            i += n
        return found

    def first_phase():
        for a in range(A):
            yield "pick", a
            yield "turn", a

    def later_phases():
        done = A
        for t in range(TILES):
            while done < LINES * (t + 1):
                yield "turn", done
                done += 1
            work = [("interact", 4 * t), ("interact", 4 * t + 1), "turn", ("interact", 4 * t + 2),
                    ("interact", 4 * t + 3), "turn", ("layer1_low", t), "turn", ("layer1_high", t), "turn",
                    ("layer2", t), ("layer3", t), "turn", "turn"]
            for w in work:
                if w != "turn":
                    yield w
                elif done < min(LINES * (t + 2), LINES * TILES):
                    yield "turn", done
                    done += 1

    order = [*first_phase(), *later_phases()]

    with ExitStack() as ctx:
        def sb(name, shape, dt=F32):
            return ctx.enter_context(nc.sbuf_tensor(name, shape, dt))

        def psum(name, shape):
            return ctx.enter_context(nc.psum_tensor(name, shape, F32))

        def sem(name):
            return ctx.enter_context(nc.semaphore(name))

        ids_sb = sb("ids_sb", [P, TILES, F], I32)
        ids_f = sb("ids_f", [P, TILES, F])
        ids_rows = sb("ids_rows", [F, B], F32R)
        dense_sb = sb("dense_sb", [P, TILES, D])
        rows = sb("rows", [P, TILES, F - A, D])
        raw = sb("raw", [K, RAW, CHUNKS, D])
        high = sb("high", [K, 2, CHUNKS, D], F32R)
        low = sb("low", [K, 2, CHUNKS, D], F32R)
        onehot = sb("onehot", [K, 2, CHUNKS, B], F32R)
        row_of = sb("row_of", [K, CHUNKS])
        minus_row_of = sb("minus_row_of", [K, CHUNKS])
        turned = sb("turned", [P, TILES, P, QP])
        pairs = sb("pairs", [P, T4, P])
        ident = sb("ident", [P, P])
        ident_r = sb("ident_r", [F, F], F32R)
        zeros = sb("zeros", [P, H1])
        w_pairs = sb("w_pairs", [P, T4, H1])
        w_dense = sb("w_dense", [P, 2, H1])
        w2 = sb("w2", [P, M1, H2])
        w3 = sb("w3", [P, M2])
        bias1 = sb("bias1", [P, M1])
        bias2 = sb("bias2", [P, M2])
        h1 = sb("h1", [P, M1, P])
        h2 = sb("h2", [P, M2, P])
        y = sb("y", [1, B])

        ps_turn = [psum(f"ps_turn{i}", [P, LINE, P]) for i in range(2)]
        ps_pairs = [psum(f"ps_pairs{i}", [P, GROUPS, SLOT]) for i in range(2)]
        ps_mlp = [psum(f"ps_mlp{i}", [P, LINE, P]) for i in range(2)]

        def bank(ps, i):
            return ps[:, i * B // P:(i + 1) * B // P, :].rearrange("p a b -> p (a b)")

        ids_dve = [bank(ps_mlp[0], 0), bank(ps_pairs[0], 1)]
        ids_act = [bank(ps_mlp[1], 0), bank(ps_pairs[1], 1)]
        ps_picked = [bank(ps_pairs[0], 0), bank(ps_pairs[1], 0)]

        ids0_loaded = sem("ids0_loaded")
        ids_loaded = sem("ids_loaded")
        dense_loaded = sem("dense_loaded")
        ident_zeroed = sem("ident_zeroed")
        constants_ready = sem("constants_ready")
        ident_r_ready = sem("ident_r_ready")
        zeros_ready = sem("zeros_ready")
        gathered = [[sem(f"gathered_{t}_{g}") for g in range(LINES)] for t in range(TILES)]
        raw_loaded = [sem(f"raw_loaded_{i}") for i in range(RAW)]
        w_pairs_zeroed = sem("w_pairs_zeroed")
        w_pairs_loaded = sem("w_pairs_loaded")
        w_dense_loaded = sem("w_dense_loaded")
        w_dense_summed = sem("w_dense_summed")
        w2_loaded = sem("w2_loaded")
        small_loaded = sem("small_loaded")
        pads_zeroed = sem("pads_zeroed")
        ids_f_ready = sem("ids_f_ready")
        ids_rows_ps = sem("ids_rows_ps")
        ids_rows_ready = sem("ids_rows_ready")
        ids_spread = sem("ids_spread")
        high_ready = sem("high_ready")
        low_ready = sem("low_ready")
        onehot_dve = sem("onehot_dve")
        distance_act = sem("distance_act")
        onehot_act = sem("onehot_act")
        picked_ps = sem("picked_ps")
        picked_act = sem("picked_act")
        picked_dve = sem("picked_dve")
        turned_ps = sem("turned_ps")
        turned_act = sem("turned_act")
        turned_dve = sem("turned_dve")
        pairs_ps = sem("pairs_ps")
        step0_act = sem("step0_act")
        step0_dve = sem("step0_dve")
        pairs_act = sem("pairs_act")
        pairs_dve = sem("pairs_dve")
        h1_ps = sem("h1_ps")
        h1_act = sem("h1_act")
        h1_dve = sem("h1_dve")
        h2_ps = sem("h2_ps")
        h2_act = sem("h2_act")
        h2_dve = sem("h2_dve")
        y_ps = sem("y_ps")
        y_ready = sem("y_ready")
        y_stored = sem("y_stored")

        def evens(n):
            return (n + 1) // 2

        def odds(n):
            return n // 2

        def copy_turned(copy, k):
            t, g = divmod(k, LINES)
            last = None
            for i, f, step, n in runs(lines[g]):
                last = copy(turned[:, t, :, AT + f:AT + f + step * (n - 1) + 1:step],
                            ps_turn[k % 2][:, i:i + n, :].rearrange("d n b -> d b n"))
            for c in range(COPIES):
                f = N - COPIES + c
                if f in lines[g]:
                    last = copy(turned[:, t, :, c], ps_turn[k % 2][:, lines[g].index(f), :])
            return last

        def copy_picked(copy, a):
            f = 1 + picked[a]
            src = ps_picked[a % 2].rearrange("d (t b) -> d t b", b=P)
            last = copy(turned[:, :, :, AT + f], src)
            if f >= N - COPIES:
                last = copy(turned[:, :, :, f - (N - COPIES)], src)
            return last

        def copy_pairs(copy, u, s, q):
            c = s * COLS + q
            b0 = u % PARTS * HB + s
            return copy(pairs[QP * q:QP * q + QP, :, b0:b0 + SAMPLES * (GROUPS - 1) + 1:SAMPLES]
                        .rearrange("i t g -> i g t"),
                        ps_pairs[u % 2][QP * s:QP * s + QP, :, c:c + Q * (T4 - 1) + 1:Q])

        def copy_last_pairs(copy, u, s):
            c = s * COLS + COLS - COPIES
            b0 = u % PARTS * HB + s
            return copy(pairs[0:COPIES, 0:COPIES, b0:b0 + SAMPLES * (GROUPS - 1) + 1:SAMPLES]
                        .rearrange("i t g -> i g t"),
                        ps_pairs[u % 2][QP * s:QP * s + COPIES, :, c:c + COPIES])

        block = ctx.enter_context(nc.Block())

        @block.sync
        def _(sp):
            def load_raw(a):
                if a >= RAW:
                    sp.wait_ge(low_ready, a - RAW + 1)
                whole = K // 16 * 16
                table = tables[picked[a]].rearrange("(p c) d -> p c d", c=CHUNKS)
                for p0, p1 in ((0, whole), (whole, K)):
                    sp.dma_start(raw[p0:p1, a % RAW, :, :], table[p0:p1]).then_inc(raw_loaded[a % RAW], 16)

            sp.dma_start(ids_sb[:, 0, :], ids[0:P, :]).then_inc(ids0_loaded, 16)
            sp.dma_start(ids_sb[:, 1:TILES, :],
                         ids[P:B, :].rearrange("(t p) f -> p t f", p=P)).then_inc(ids_loaded, 16)
            load_raw(0)
            load_raw(1)
            sp.dma_start(dense_sb[:, :, :], dense.rearrange("(t p) d -> p t d", p=P)).then_inc(dense_loaded, 16)
            load_raw(2)
            sp.dma_start(w_dense[:, 0, :], W1[0:D, :]).then_inc(w_dense_loaded, 16)
            sp.dma_start(w_dense[:, 1, :], W1[W1.shape[0] - D:W1.shape[0], :]).then_inc(w_dense_loaded, 16)
            sp.dma_start(w2[:, :, :], W2.rearrange("(k p) n -> p k n", p=P)).then_inc(w2_loaded, 16)
            load_raw(3)
            sp.wait_ge(w_pairs_zeroed, 1)
            for j in range(COLS - COPIES):
                q, t4 = j % Q, j // Q
                r = first_pair_row(j)
                sp.dma_start(w_pairs[QP * q + AT + j + 1:QP * q + AT + N, t4, :],
                             W1[r:r + N - 1 - j, :]).then_inc(w_pairs_loaded, 16)
                if j % 5 == 4 and 4 + j // 5 < A:
                    load_raw(4 + j // 5)
            for c in range(COPIES):
                r = first_pair_row(COLS - COPIES + c)
                sp.dma_start(w_pairs[c:COPIES, c, :], W1[r:r + COPIES - c, :]).then_inc(w_pairs_loaded, 16)
            with nc.allow_non_contiguous_dma(reason="biases and the last weights, one value per partition"):
                sp.dma_start(bias1[:, :], b1.rearrange("(m p) -> p m", p=P)).then_inc(small_loaded, 16)
                sp.dma_start(bias2[:, :], b2.rearrange("(m p) -> p m", p=P)).then_inc(small_loaded, 16)
                sp.dma_start(w3[:, :], W3.rearrange("(m p) o -> p (m o)", p=P)).then_inc(small_loaded, 16)
            sp.wait_ge(y_ready, TILES)
            sp.dma_start(out.rearrange("b o -> o b"), y[:, :]).then_inc(y_stored, 16)
            sp.wait_ge(y_stored, 16)

        @block.gpsimd
        def _(pool):
            nc.gpsimd.memset(ident[:, :], 0.0).then_inc(ident_zeroed, 1)
            pool.wait_ge(ident_zeroed, 1)
            nc.gpsimd.affine_select(out=ident[:, :], in_=ident[:, :], compare_op=ALU.not_equal, fill=1.0,
                                    base=0, pattern=[[-1, P]], channel_multiplier=1).then_inc(constants_ready, 1)
            nc.gpsimd.iota(row_of[:, :], [[1, CHUNKS]], base=0, channel_multiplier=CHUNKS,
                           allow_small_or_imprecise_dtypes=True).then_inc(constants_ready, 1)
            nc.gpsimd.iota(minus_row_of[:, :], [[-1, CHUNKS]], base=0, channel_multiplier=-CHUNKS,
                           allow_small_or_imprecise_dtypes=True).then_inc(constants_ready, 1)
            for t in range(TILES):
                if t == 0:
                    pool.wait_ge(ids0_loaded, 16)
                if t == 1:
                    pool.wait_ge(ids_loaded, 16)
                for i, f in enumerate(gathered_tables):
                    pool.indirect_dma_start(
                        rows[:, t, i, :], None, tables[f],
                        bass.IndirectOffsetOnAxis(ids_sb[:, t, f:f + 1], 0),
                    ).then_inc(gathered[t][(1 + i) // LINE], 16)

        @block.tensor
        def _(pe):
            def turn_ids():
                pe.wait_ge(constants_ready, 1)
                pe.wait_ge(ids_f_ready, 1)
                for t in range(TILES):
                    mm = pe.transpose(ps_mlp[0][0:F, t, :], ids_f[:, t, :], ident[:, :])
                mm.then_inc(ids_rows_ps, 1)

            def spread_ids(a):
                f = picked[a]
                if a == 0:
                    pe.wait_ge(ident_r_ready, 1)
                    pe.wait_ge(ids_rows_ready, 1)
                if a >= 2:
                    pe.wait_ge(onehot_dve, 2 * (a - 1))
                    pe.wait_ge(distance_act, a - 1)
                for o in (ids_dve[a % 2], ids_act[a % 2]):
                    mm = pe.matmul(o[0:K, :], ident_r[:, f:f + 1].to_broadcast([F, K]), ids_rows[:, :],
                                   start=True, stop=True)
                mm.then_inc(ids_spread, 1)

            def pick(a):
                pe.wait_ge(high_ready, a + 1)
                pe.wait_ge(low_ready, a + 1)
                if a >= 2:
                    if a % 2 == 0:
                        pe.wait_ge(picked_dve, evens(a - 1))
                    else:
                        pe.wait_ge(picked_act, odds(a - 1))
                for c in range(CHUNKS):
                    if c == 0:
                        pe.wait_ge(onehot_dve, 2 * a + 1)
                    elif c == DVE_CHUNKS[0]:
                        pe.wait_ge(onehot_dve, 2 * a + 2)
                    elif c == DVE_CHUNKS[1]:
                        pe.wait_ge(onehot_act, a + 1)
                    for part in (high, low):
                        mm = pe.matmul(ps_picked[a % 2], part[:, a % 2, c, :], onehot[:, a % 2, c, :],
                                       start=(c == 0 and part is high), stop=(c == CHUNKS - 1 and part is low))
                mm.then_inc(picked_ps, 1)

            def turn(k):
                t, g = divmod(k, LINES)
                if k == 0:
                    pe.wait_ge(dense_loaded, 16)
                pe.wait_ge(gathered[t][g], 16 * (len(lines[g]) - (g == 0)))
                if k >= 2:
                    if k % 2 == 0:
                        pe.wait_ge(turned_act, evens(k - 1))
                    else:
                        pe.wait_ge(turned_dve, odds(k - 1))
                for i, f in enumerate(lines[g]):
                    src = dense_sb[:, t, :] if f == 0 else rows[:, t, LINE * g + i - 1, :]
                    mm = pe.transpose(ps_turn[k % 2][:, i, :], src, ident[:, :])
                mm.then_inc(turned_ps, 1)

            def interact(u):
                t, part = divmod(u, PARTS)
                if part == 0:
                    if t == 0:
                        pe.wait_ge(pads_zeroed, 1)
                        pe.wait_ge(picked_dve, evens(A))
                        pe.wait_ge(picked_act, odds(A))
                    pe.wait_ge(turned_act, evens(LINES * (t + 1)))
                    pe.wait_ge(turned_dve, odds(LINES * (t + 1)))
                if u >= 2:
                    pe.wait_ge(pairs_act, u - 1)
                    pe.wait_ge(pairs_dve, u - 1)
                for g in range(GROUPS):
                    b0 = part * HB + SAMPLES * g
                    four = turned[:, t, b0:b0 + SAMPLES, :]
                    mm = pe.matmul(ps_pairs[u % 2][:, g, 0:SAMPLES * COLS], four.rearrange("d s n -> d (s n)"),
                                   four[:, :, AT:AT + COLS], start=True, stop=True)
                mm.then_inc(pairs_ps, 1)

            def layer1_out(m):
                return ps_mlp[m // 2][:, m % 2, :]

            def layer1_low(t):
                if t == 0:
                    pe.wait_ge(w_dense_summed, 1)
                else:
                    pe.wait_ge(y_ready, t)
                for m in range(M1):
                    pe.matmul(layer1_out(m), w_dense[:, 0, m * P:m * P + P], turned[:, t, :, AT],
                              start=(m % 2 == 0), stop=False, skip_group_check=True)
                if t == 0:
                    pe.wait_ge(w_pairs_loaded, 16 * COLS)
                pe.wait_ge(pairs_act, PARTS * (t + 1))
                pe.wait_ge(pairs_dve, PARTS * (t + 1))
                layer1_pairs(range(0, M1 // 2))

            def layer1_pairs(ms):
                for m in ms:
                    for t4 in range(T4):
                        mm = pe.matmul(layer1_out(m), w_pairs[:, t4, m * P:m * P + P], pairs[:, t4, :],
                                       start=False, stop=(t4 == T4 - 1), skip_group_check=True)
                mm.then_inc(h1_ps, 1)

            def layer2(t):
                if t == 0:
                    pe.wait_ge(w2_loaded, 16)
                pe.wait_ge(h1_act, t + 1)
                for m in range(M2):
                    for k in range(M1):
                        if m == 0 and k == M1 // 2:
                            pe.wait_ge(h1_dve, t + 1)
                        mm = pe.matmul(ps_mlp[m][:, 2, :], w2[:, k, m * P:m * P + P], h1[:, k, :],
                                       start=(k == 0), stop=(k == M1 - 1))
                    mm.then_inc(h2_ps, 1)

            def layer3(t):
                if t == 0:
                    pe.wait_ge(small_loaded, 48)
                pe.wait_ge(h2_act, t + 1)
                for k in range(M2):
                    if k == 1:
                        pe.wait_ge(h2_dve, t + 1)
                    mm = pe.matmul(ps_mlp[0][0:1, 3, :], w3[:, k:k + 1], h2[:, k, :],
                                   start=(k == 0), stop=(k == M2 - 1))
                mm.then_inc(y_ps, 1)

            turn_ids()
            spread_ids(0)
            for what, n in order:
                if what == "pick":
                    if n + 1 < A:
                        spread_ids(n + 1)
                    pick(n)
                elif what == "turn":
                    turn(n)
                elif what == "interact":
                    interact(n)
                elif what == "layer1_low":
                    layer1_low(n)
                elif what == "layer1_high":
                    layer1_pairs(range(M1 // 2, M1))
                elif what == "layer2":
                    layer2(n)
                else:
                    layer3(n)

        @block.scalar
        def _(act):
            def copy(dst, src):
                return nc.scalar.activation(dst, src, ACT.Copy)

            def split_high(a):
                act.wait_ge(raw_loaded[a % RAW], 32 * (a // RAW + 1))
                if a >= 2:
                    act.wait_ge(picked_ps, a - 1)
                copy(high[:, a % 2, :, :], raw[:, a % RAW, :, :]).then_inc(high_ready, 1)

            def onehot_rest(a):
                act.wait_ge(ids_spread, a + 1)
                if a >= 2:
                    act.wait_ge(picked_ps, a - 1)
                for c in range(DVE_CHUNKS[1], CHUNKS):
                    last = nc.scalar.activation(onehot[:, a % 2, c, :], ids_act[a % 2][0:K, :], ACT.Abs,
                                                bias=minus_row_of[:, c:c + 1])
                last.then_inc(distance_act, 1)
                act.wait_ge(distance_act, a + 1)
                part = onehot[:, a % 2, DVE_CHUNKS[1]:CHUNKS, :]
                nc.scalar.activation(part, part.bitcast(F32), ACT.Relu, bias=1.0, scale=-1.0).then_inc(onehot_act, 1)

            act.wait_ge(zeros_ready, 1)
            copy(w_pairs[:, :, :], zeros[:, :].unsqueeze(1).to_broadcast([P, T4, H1])).then_inc(w_pairs_zeroed, 1)
            act.wait_ge(constants_ready, 3)
            split_high(0)
            onehot_rest(0)
            for what, n in order:
                if what == "pick":
                    if n + 1 < A:
                        split_high(n + 1)
                        onehot_rest(n + 1)
                    if n % 2 == 1:
                        act.wait_ge(picked_ps, n + 1)
                        copy_picked(copy, n).then_inc(picked_act, 1)
                    if n == A - 1:
                        pads = turned[:, :, :, AT + N:QP].rearrange("p t b n -> p (t b) n")
                        copy(pads, zeros[:, 0:B].unsqueeze(2).to_broadcast([P, B, QP - AT - N])).then_inc(pads_zeroed, 1)
                elif what == "turn":
                    if n % 2 == 0:
                        act.wait_ge(turned_ps, n + 1)
                        copy_turned(copy, n).then_inc(turned_act, 1)
                elif what == "interact":
                    act.wait_ge(pairs_ps, n + 1)
                    for s in range(0, SAMPLES // 2):
                        last = copy_pairs(copy, n, s, 0)
                    last.then_inc(step0_act, 1)
                    for s in range(0, SAMPLES // 2):
                        for q in range(1, Q):
                            copy_pairs(copy, n, s, q)
                    act.wait_ge(step0_act, n + 1)
                    for s in range(0, SAMPLES // 2):
                        last = copy_last_pairs(copy, n, s)
                    last.then_inc(pairs_act, 1)
                elif what == "layer1_high":
                    if n == 0:
                        act.wait_ge(small_loaded, 48)
                    act.wait_ge(h1_ps, 2 * n + 1)
                    for m in range(0, M1 // 2):
                        last = nc.scalar.activation(h1[:, m, :], ps_mlp[0][:, m, :], ACT.Relu, bias=bias1[:, m:m + 1])
                    last.then_inc(h1_act, 1)
                elif what == "layer2":
                    act.wait_ge(h2_ps, M2 * n + 1)
                    nc.scalar.activation(h2[:, 0, :], ps_mlp[0][:, 2, :], ACT.Relu,
                                         bias=bias2[:, 0:1]).then_inc(h2_act, 1)

        @block.vector
        def _(dve):
            def copy(dst, src):
                return nc.vector.tensor_copy(dst, src)

            def split_low(a):
                dve.wait_ge(high_ready, a + 1)
                nc.vector.tensor_tensor(low[:, a % 2, :, :], raw[:, a % RAW, :, :], high[:, a % 2, :, :].bitcast(F32),
                                        ALU.subtract).then_inc(low_ready, 1)

            def onehot_first(a):
                dve.wait_ge(ids_spread, a + 1)
                if a >= 2:
                    dve.wait_ge(picked_ps, a - 1)
                c0 = 0
                for c1 in DVE_CHUNKS:
                    n = [K, c1 - c0, B]
                    nc.vector.tensor_tensor(onehot[:, a % 2, c0:c1, :],
                                            ids_dve[a % 2][0:K, :].unsqueeze(1).to_broadcast(n),
                                            row_of[:, c0:c1].unsqueeze(2).to_broadcast(n),
                                            ALU.is_equal).then_inc(onehot_dve, 1)
                    c0 = c1

            nc.vector.memset(zeros[:, :], 0.0).then_inc(zeros_ready, 1)
            dve.wait_ge(constants_ready, 3)
            copy(ident_r[:, :], ident[0:F, 0:F]).then_inc(ident_r_ready, 1)
            dve.wait_ge(ids0_loaded, 16)
            dve.wait_ge(ids_loaded, 16)
            copy(ids_f[:, :, :], ids_sb[:, :, :]).then_inc(ids_f_ready, 1)
            dve.wait_ge(ids_rows_ps, 1)
            copy(ids_rows[:, :], ps_mlp[0][0:F, :, :].rearrange("f t b -> f (t b)")).then_inc(ids_rows_ready, 1)
            onehot_first(0)
            split_low(0)
            for what, n in order:
                if what == "pick":
                    if n + 1 < A:
                        onehot_first(n + 1)
                        split_low(n + 1)
                    if n % 2 == 0:
                        dve.wait_ge(picked_ps, n + 1)
                        copy_picked(copy, n).then_inc(picked_dve, 1)
                    if n == A - 1:
                        dve.wait_ge(w_dense_loaded, 32)
                        nc.vector.tensor_tensor(w_dense[:, 0, :], w_dense[:, 0, :], w_dense[:, 1, :],
                                                ALU.add).then_inc(w_dense_summed, 1)
                elif what == "turn":
                    if n % 2 == 1:
                        dve.wait_ge(turned_ps, n + 1)
                        copy_turned(copy, n).then_inc(turned_dve, 1)
                elif what == "interact":
                    dve.wait_ge(pairs_ps, n + 1)
                    for s in range(SAMPLES // 2, SAMPLES):
                        last = copy_pairs(copy, n, s, 0)
                    last.then_inc(step0_dve, 1)
                    for s in range(SAMPLES // 2, SAMPLES):
                        for q in range(1, Q):
                            copy_pairs(copy, n, s, q)
                    dve.wait_ge(step0_dve, n + 1)
                    for s in range(SAMPLES // 2, SAMPLES):
                        last = copy_last_pairs(copy, n, s)
                    last.then_inc(pairs_dve, 1)
                elif what == "layer1_high":
                    if n == 0:
                        dve.wait_ge(small_loaded, 48)
                    dve.wait_ge(h1_ps, 2 * n + 2)
                    for m in range(M1 // 2, M1):
                        last = nc.vector.tensor_scalar(h1[:, m, :], ps_mlp[1][:, m % 2, :], bias1[:, m:m + 1], 0.0,
                                                       ALU.add, ALU.max)
                    last.then_inc(h1_dve, 1)
                elif what == "layer2":
                    dve.wait_ge(h2_ps, M2 * n + 2)
                    nc.vector.tensor_scalar(h2[:, 1, :], ps_mlp[1][:, 2, :], bias2[:, 1:2], 0.0,
                                            ALU.add, ALU.max).then_inc(h2_dve, 1)
                elif what == "layer3":
                    dve.wait_ge(y_ps, n + 1)
                    copy(y[:, n * P:n * P + P], ps_mlp[0][0:1, 3, :]).then_inc(y_ready, 1)


_TABLES = 26
_INS = (["r_dense_features", "ids"] + [f"tbl_{i}" for i in range(_TABLES)]
        + ["W_top1", "b_top1", "W_top2", "b_top2", "W_top3"])


def kernel(**inputs):
    import numpy as _np
    import concourse.bacc as _bacc
    from concourse import mybir as _mybir
    from concourse.bass_utils import run_bass_kernel_spmd as _run

    nc = _bacc.Bacc("TRN2", target_bir_lowering=False, num_devices=1)
    arrays, args = {}, {}
    for name in _INS:
        a = _np.ascontiguousarray(inputs[name])
        arrays[f"in_{name}_dram"] = a
        args[name] = nc.dram_tensor(f"in_{name}_dram", a.shape, _mybir.dt.from_np(a.dtype), kind="ExternalInput").ap()
    out = nc.dram_tensor("out_dram", (inputs["ids"].shape[0], 1), _mybir.dt.float32, kind="ExternalOutput").ap()
    dlrm_tower(nc, args["r_dense_features"], args["ids"], [args[f"tbl_{i}"] for i in range(_TABLES)],
               args["W_top1"], args["b_top1"], args["W_top2"], args["b_top2"], args["W_top3"], out)
    r = _run(nc, [arrays], core_ids=[0])
    return r.results[0]["out_dram"]
```
